# Optimizing a Trainium2 kernel written in Bass

```python
import numpy as np
import jax
import jax.numpy as jnp

def _softmax(x, axis=-1):
    return jax.nn.softmax(x, axis=axis)

def _gelu(x):
    return jax.nn.gelu(x, approximate=True)

def _silu(x):
    return jax.nn.silu(x)

def _sigmoid(x):
    return jax.nn.sigmoid(x)

def _layernorm(x, axis=-1, eps=1e-05):
    m = jnp.mean(x, axis=axis, keepdims=True)
    v = jnp.var(x, axis=axis, keepdims=True)
    return (x - m) / jnp.sqrt(v + eps)

def _scatter_add(tgt, idx, src, axis=0):
    return tgt.at[idx].add(src)

def _segment_sum(src, seg, n):
    return jax.ops.segment_sum(src, seg, n)
kernel_name = 'mk_gnn_preln_d4_gnn_r16_48b6d7'

def setup_inputs(seed: int=0):
    np.random.seed(seed)
    _w = jnp.asarray

    def _rec_inputs():
        import jax
        import jax.numpy as jnp
        _gk = jax.random.key(seed)
        x = -0.0003713 + 1 * jax.random.normal(jax.random.fold_in(_gk, 1), (6250, 128), jnp.float32)
        _s = jax.random.randint(jax.random.fold_in(_gk, 2), (50000,), 0, 6250, jnp.int32)
        _d = jax.random.randint(jax.random.fold_in(_gk, 3), (50000,), 0, 6250, jnp.int32)
        _loop = jnp.arange(6250, dtype=jnp.int32)
        src = jnp.concatenate([_s, _d, _loop])
        dst = jnp.concatenate([_d, _s, _loop])
        _o = jnp.argsort(dst, stable=True)
        src = src[_o]
        dst = dst[_o]
        edge_weight = 0.00149426 + 0.999557 * jax.random.normal(jax.random.fold_in(_gk, 13), (106250,), jnp.float32)
        return (x, src, dst, edge_weight)
    x, src, dst, edge_weight = _rec_inputs()

    def _L0_gnn_setup():
        import jax, jax.numpy as jnp
        import numpy as np
        N, E, K, H, L = (6250, 3125, 31250, 128, 2)
        EPS = 1e-05
        NEG_SLOPE = 0.2

        def _conv_layer(x, he_attr, row, col, stoich, W, att, bias):
            xt = x @ W
            et = he_attr @ W
            a = xt[row] @ att[:H] + et[col] @ att[H:]
            a = jax.nn.leaky_relu(a, NEG_SLOPE)
            amax = jax.ops.segment_max(a, col, num_segments=E)
            ex = jnp.exp(a - amax[col])
            den = jax.ops.segment_sum(ex, col, num_segments=E)
            alpha = ex / den[col]
            asto = jnp.abs(stoich)
            D = jax.ops.segment_sum(asto, row, num_segments=N)
            Dinv = jnp.where(D > 0, 1.0 / D, 0.0)
            B = jax.ops.segment_sum(asto, col, num_segments=E)
            Binv = jnp.where(B > 0, 1.0 / B, 0.0)
            m1 = (Binv[col] * stoich * alpha)[:, None] * xt[row]
            eout = jax.ops.segment_sum(m1, col, num_segments=E)
            m2 = (Dinv[row] * stoich * alpha)[:, None] * eout[col]
            nout = jax.ops.segment_sum(m2, row, num_segments=N)
            return nout + bias

        def _layernorm(x, gamma, beta):
            mu = jnp.mean(x, axis=-1, keepdims=True)
            var = jnp.var(x, axis=-1, keepdims=True)
            return (x - mu) * jax.lax.rsqrt(var + EPS) * gamma + beta
        key = jax.random.key(seed)
        ks = jax.random.split(key, 10)
        s = 1.0 / np.sqrt(H)
        return {'metabolite_embeddings': jax.random.normal(ks[0], (N, H), jnp.float32), 'hyperedge_index': jnp.stack([jax.random.randint(ks[1], (K,), 0, N, jnp.int32), jax.random.randint(ks[2], (K,), 0, E, jnp.int32)]), 'stoichiometry': jax.random.normal(ks[3], (K,), jnp.float32), 'reaction_features': jax.random.normal(ks[4], (E, H), jnp.float32), 'W': jax.random.normal(ks[5], (L, H, H), jnp.float32) * s, 'att': jax.random.normal(ks[6], (L, 2 * H), jnp.float32) * s, 'bias': jnp.zeros((L, H), jnp.float32), 'gamma': jnp.ones((L, H), jnp.float32), 'beta': jnp.zeros((L, H), jnp.float32)}
    _L0_gnn_all = _L0_gnn_setup()
    _L0_gnn_in = {k: v for k, v in _L0_gnn_all.items() if k in ('reaction_features', 'W', 'att', 'bias', 'gamma', 'beta')}
    del _L0_gnn_all

    def _L1_gnn_setup():
        import jax, jax.numpy as jnp
        import numpy as np
        N, E, D = (3125, 50000, 128)
        key = jax.random.key(seed)
        ks = jax.random.split(key, 10)
        s = 1.0 / np.sqrt(2 * D)
        t = 1.0 / np.sqrt(D)
        return {'x': jax.random.normal(ks[0], (N, D), dtype=jnp.float32), 'edge_index': jax.random.randint(ks[1], (2, E), 0, N, dtype=jnp.int64), 'mW1': jax.random.uniform(ks[2], (2 * D, D), jnp.float32, -s, s), 'mb1': jax.random.uniform(ks[3], (D,), jnp.float32, -s, s), 'mW2': jax.random.uniform(ks[4], (D, D), jnp.float32, -t, t), 'mb2': jax.random.uniform(ks[5], (D,), jnp.float32, -t, t), 'uW1': jax.random.uniform(ks[6], (2 * D, D), jnp.float32, -s, s), 'ub1': jax.random.uniform(ks[7], (D,), jnp.float32, -s, s), 'uW2': jax.random.uniform(ks[8], (D, D), jnp.float32, -t, t), 'ub2': jax.random.uniform(ks[9], (D,), jnp.float32, -t, t)}
    _L1_gnn_all = _L1_gnn_setup()
    _L1_gnn_in = {k: v for k, v in _L1_gnn_all.items() if k in ('mW1', 'mb1', 'mW2', 'mb2', 'uW1', 'ub1', 'uW2', 'ub2')}
    del _L1_gnn_all

    def _L2_gnn_setup():
        import jax, jax.numpy as jnp
        import numpy as np
        N, E, DIN, H, DOUT = (6250, 25000, 128, 128, 128)
        LN_EPS = 1e-05

        def _layernorm(x, g, b):
            m = jnp.mean(x, axis=-1, keepdims=True)
            v = jnp.mean((x - m) ** 2, axis=-1, keepdims=True)
            return (x - m) * jax.lax.rsqrt(v + LN_EPS) * g + b
        key = jax.random.key(seed)
        ks = jax.random.split(key, 24)
        s = 1.0 / np.sqrt(H)
        inp = {'feat': jax.random.normal(ks[0], (N, DIN), jnp.float32), 'edge_src': jax.random.randint(ks[1], (E,), 0, N, jnp.int32), 'edge_dst': jax.random.randint(ks[2], (E,), 0, N, jnp.int32), 'W_src': jax.random.normal(ks[3], (DIN, H), jnp.float32) * s, 'b_src': jax.random.normal(ks[4], (H,), jnp.float32) * s, 'W_dst': jax.random.normal(ks[5], (DIN, H), jnp.float32) * s, 'b_dst': jax.random.normal(ks[6], (H,), jnp.float32) * s, 'W1a': jax.random.normal(ks[7], (H, H), jnp.float32) * s, 'W1b': jax.random.normal(ks[8], (H, H), jnp.float32) * s, 'b1': jax.random.normal(ks[9], (H,), jnp.float32) * s, 'W2': jax.random.normal(ks[10], (H, H), jnp.float32) * s, 'b2': jax.random.normal(ks[11], (H,), jnp.float32) * s, 'W3': jax.random.normal(ks[12], (H, H), jnp.float32) * s, 'b3': jax.random.normal(ks[13], (H,), jnp.float32) * s, 'ln_g': jnp.ones((H,), jnp.float32), 'ln_b': jnp.zeros((H,), jnp.float32), 'Wg1a': jax.random.normal(ks[14], (H, H), jnp.float32) * s, 'Wg1b': jax.random.normal(ks[15], (H, H), jnp.float32) * s, 'bg1': jax.random.normal(ks[16], (H,), jnp.float32) * s, 'Wg2': jax.random.normal(ks[17], (H, 1), jnp.float32) * s, 'bg2': jax.random.normal(ks[18], (1,), jnp.float32) * s, 'W_out': jax.random.normal(ks[19], (H, DOUT), jnp.float32) * s, 'b_out': jax.random.normal(ks[20], (DOUT,), jnp.float32) * s}
        return inp
    _L2_gnn_all = _L2_gnn_setup()
    _L2_gnn_in = {k: v for k, v in _L2_gnn_all.items() if k in ('W_src', 'b_src', 'W_dst', 'b_dst', 'W1a', 'W1b', 'b1', 'W2', 'b2', 'W3', 'b3', 'ln_g', 'ln_b', 'Wg1a', 'Wg1b', 'bg1', 'Wg2', 'bg2', 'W_out', 'b_out')}
    del _L2_gnn_all

    def _L3_gnn_setup():
        import jax, jax.numpy as jnp
        import numpy as np
        N, F_IN, C_OUT, H = (3125, 128, 32, 4)
        ALPHA = 0.5
        SLOPE = 0.2

        def _gat_conv(x, W, a_src, a_dst, b, src, dst):
            n = x.shape[0]
            h = (x @ W).reshape(n, H, C_OUT)
            e_src = jnp.sum(h * a_src[None], -1)
            e_dst = jnp.sum(h * a_dst[None], -1)
            e = jax.nn.leaky_relu(e_src[src] + e_dst[dst], SLOPE)
            m = jax.ops.segment_max(e, dst, num_segments=n)
            ex = jnp.exp(e - m[dst])
            denom = jax.ops.segment_sum(ex, dst, num_segments=n)
            att = ex / denom[dst]
            msg = h[src] * att[:, :, None]
            out = jax.ops.segment_sum(msg, dst, num_segments=n)
            return out.reshape(n, H * C_OUT) + b
        key = jax.random.key(seed)
        ks = jax.random.split(key, 12)
        x = jax.random.normal(ks[0], (N, F_IN), dtype=jnp.float32)
        edge_index = jax.random.randint(ks[1], (2, 100000), 0, N, dtype=jnp.int64)

        def gat_params(k):
            k1, k2, k3, k4 = jax.random.split(k, 4)
            W = jax.random.normal(k1, (F_IN, H * C_OUT), dtype=jnp.float32) * 0.1
            a_src = jax.random.normal(k2, (H, C_OUT), dtype=jnp.float32) * 0.1
            a_dst = jax.random.normal(k3, (H, C_OUT), dtype=jnp.float32) * 0.1
            b = jax.random.normal(k4, (H * C_OUT,), dtype=jnp.float32) * 0.1
            return (W, a_src, a_dst, b)
        W1, a_src1, a_dst1, b1 = gat_params(ks[2])
        W2, a_src2, a_dst2, b2 = gat_params(ks[3])
        return {'x': x, 'edge_index': edge_index, 'W1': W1, 'a_src1': a_src1, 'a_dst1': a_dst1, 'b1': b1, 'W2': W2, 'a_src2': a_src2, 'a_dst2': a_dst2, 'b2': b2}
    _L3_gnn_all = _L3_gnn_setup()
    _L3_gnn_in = {k: v for k, v in _L3_gnn_all.items() if k in ('W1', 'a_src1', 'a_dst1', 'b1', 'W2', 'a_src2', 'a_dst2', 'b2')}
    del _L3_gnn_all
    return {'x': x, 'src': src, 'dst': dst, 'edge_weight': edge_weight, 'L0_gnn_reaction_features': _L0_gnn_in['reaction_features'], 'L0_gnn_W': _L0_gnn_in['W'], 'L0_gnn_att': _L0_gnn_in['att'], 'L0_gnn_bias': _L0_gnn_in['bias'], 'L0_gnn_gamma': _L0_gnn_in['gamma'], 'L0_gnn_beta': _L0_gnn_in['beta'], 'L1_gnn_mW1': _L1_gnn_in['mW1'], 'L1_gnn_mb1': _L1_gnn_in['mb1'], 'L1_gnn_mW2': _L1_gnn_in['mW2'], 'L1_gnn_mb2': _L1_gnn_in['mb2'], 'L1_gnn_uW1': _L1_gnn_in['uW1'], 'L1_gnn_ub1': _L1_gnn_in['ub1'], 'L1_gnn_uW2': _L1_gnn_in['uW2'], 'L1_gnn_ub2': _L1_gnn_in['ub2'], 'L2_gnn_W_src': _L2_gnn_in['W_src'], 'L2_gnn_b_src': _L2_gnn_in['b_src'], 'L2_gnn_W_dst': _L2_gnn_in['W_dst'], 'L2_gnn_b_dst': _L2_gnn_in['b_dst'], 'L2_gnn_W1a': _L2_gnn_in['W1a'], 'L2_gnn_W1b': _L2_gnn_in['W1b'], 'L2_gnn_b1': _L2_gnn_in['b1'], 'L2_gnn_W2': _L2_gnn_in['W2'], 'L2_gnn_b2': _L2_gnn_in['b2'], 'L2_gnn_W3': _L2_gnn_in['W3'], 'L2_gnn_b3': _L2_gnn_in['b3'], 'L2_gnn_ln_g': _L2_gnn_in['ln_g'], 'L2_gnn_ln_b': _L2_gnn_in['ln_b'], 'L2_gnn_Wg1a': _L2_gnn_in['Wg1a'], 'L2_gnn_Wg1b': _L2_gnn_in['Wg1b'], 'L2_gnn_bg1': _L2_gnn_in['bg1'], 'L2_gnn_Wg2': _L2_gnn_in['Wg2'], 'L2_gnn_bg2': _L2_gnn_in['bg2'], 'L2_gnn_W_out': _L2_gnn_in['W_out'], 'L2_gnn_b_out': _L2_gnn_in['b_out'], 'L3_gnn_W1': _L3_gnn_in['W1'], 'L3_gnn_a_src1': _L3_gnn_in['a_src1'], 'L3_gnn_a_dst1': _L3_gnn_in['a_dst1'], 'L3_gnn_b1': _L3_gnn_in['b1'], 'L3_gnn_W2': _L3_gnn_in['W2'], 'L3_gnn_a_src2': _L3_gnn_in['a_src2'], 'L3_gnn_a_dst2': _L3_gnn_in['a_dst2'], 'L3_gnn_b2': _L3_gnn_in['b2']}

def reference(x, src, dst, edge_weight, L0_gnn_reaction_features, L0_gnn_W, L0_gnn_att, L0_gnn_bias, L0_gnn_gamma, L0_gnn_beta, L1_gnn_mW1, L1_gnn_mb1, L1_gnn_mW2, L1_gnn_mb2, L1_gnn_uW1, L1_gnn_ub1, L1_gnn_uW2, L1_gnn_ub2, L2_gnn_W_src, L2_gnn_b_src, L2_gnn_W_dst, L2_gnn_b_dst, L2_gnn_W1a, L2_gnn_W1b, L2_gnn_b1, L2_gnn_W2, L2_gnn_b2, L2_gnn_W3, L2_gnn_b3, L2_gnn_ln_g, L2_gnn_ln_b, L2_gnn_Wg1a, L2_gnn_Wg1b, L2_gnn_bg1, L2_gnn_Wg2, L2_gnn_bg2, L2_gnn_W_out, L2_gnn_b_out, L3_gnn_W1, L3_gnn_a_src1, L3_gnn_a_dst1, L3_gnn_b1, L3_gnn_W2, L3_gnn_a_src2, L3_gnn_a_dst2, L3_gnn_b2):
    import jax
    import jax.numpy as jnp

    def _L0_gnn_ref(metabolite_embeddings, hyperedge_index, stoichiometry, reaction_features, W, att, bias, gamma, beta):
        import jax, jax.numpy as jnp
        import numpy as np
        N, E, K, H, L = (6250, 3125, 31250, 128, 2)
        EPS = 1e-05
        NEG_SLOPE = 0.2

        def _conv_layer(x, he_attr, row, col, stoich, W, att, bias):
            xt = x @ W
            et = he_attr @ W
            a = xt[row] @ att[:H] + et[col] @ att[H:]
            a = jax.nn.leaky_relu(a, NEG_SLOPE)
            amax = jax.ops.segment_max(a, col, num_segments=E)
            ex = jnp.exp(a - amax[col])
            den = jax.ops.segment_sum(ex, col, num_segments=E)
            alpha = ex / den[col]
            asto = jnp.abs(stoich)
            D = jax.ops.segment_sum(asto, row, num_segments=N)
            Dinv = jnp.where(D > 0, 1.0 / D, 0.0)
            B = jax.ops.segment_sum(asto, col, num_segments=E)
            Binv = jnp.where(B > 0, 1.0 / B, 0.0)
            m1 = (Binv[col] * stoich * alpha)[:, None] * xt[row]
            eout = jax.ops.segment_sum(m1, col, num_segments=E)
            m2 = (Dinv[row] * stoich * alpha)[:, None] * eout[col]
            nout = jax.ops.segment_sum(m2, row, num_segments=N)
            return nout + bias

        def _layernorm(x, gamma, beta):
            mu = jnp.mean(x, axis=-1, keepdims=True)
            var = jnp.var(x, axis=-1, keepdims=True)
            return (x - mu) * jax.lax.rsqrt(var + EPS) * gamma + beta
        row, col = (hyperedge_index[0], hyperedge_index[1])
        x = metabolite_embeddings
        for l in range(L):
            out = _conv_layer(x, reaction_features, row, col, stoichiometry, W[l], att[l], bias[l])
            out = _layernorm(out, gamma[l], beta[l])
            x = jnp.tanh(out + x)
        return x

    def _L1_gnn_ref(x, edge_index, mW1, mb1, mW2, mb2, uW1, ub1, uW2, ub2):
        import jax, jax.numpy as jnp
        import numpy as np
        N, E, D = (3125, 50000, 128)
        row, col = (edge_index[0], edge_index[1])
        msg_in = jnp.concatenate([x[row], x[col]], axis=-1)
        h = jax.nn.relu(msg_in @ mW1 + mb1)
        messages = h @ mW2 + mb2
        aggregated = jax.ops.segment_sum(messages, col, num_segments=x.shape[0])
        upd_in = jnp.concatenate([x, aggregated], axis=-1)
        g = jax.nn.relu(upd_in @ uW1 + ub1)
        return jax.nn.relu(g @ uW2 + ub2)

    def _L2_gnn_ref(feat, edge_src, edge_dst, W_src, b_src, W_dst, b_dst, W1a, W1b, b1, W2, b2, W3, b3, ln_g, ln_b, Wg1a, Wg1b, bg1, Wg2, bg2, W_out, b_out):
        import jax, jax.numpy as jnp
        import numpy as np
        N, E, DIN, H, DOUT = (6250, 25000, 128, 128, 128)
        LN_EPS = 1e-05

        def _layernorm(x, g, b):
            m = jnp.mean(x, axis=-1, keepdims=True)
            v = jnp.mean((x - m) ** 2, axis=-1, keepdims=True)
            return (x - m) * jax.lax.rsqrt(v + LN_EPS) * g + b
        gelu = lambda x: jax.nn.gelu(x, approximate=False)
        src_h = feat @ W_src + b_src
        dst_h = feat @ W_dst + b_dst
        se = src_h[edge_src]
        de = dst_h[edge_dst]
        h = gelu(se @ W1a + de @ W1b + b1)
        h = gelu(h @ W2 + b2)
        msg = _layernorm(h @ W3 + b3, ln_g, ln_b)
        gate = jax.nn.sigmoid(gelu(se @ Wg1a + de @ Wg1b + bg1) @ Wg2 + bg2)
        msg = gate * msg
        upd = jax.ops.segment_sum(msg, edge_dst, num_segments=N)
        return upd @ W_out + b_out

    def _L3_gnn_ref(x, edge_index, W1, a_src1, a_dst1, b1, W2, a_src2, a_dst2, b2):
        import jax, jax.numpy as jnp
        import numpy as np
        N, F_IN, C_OUT, H = (3125, 128, 32, 4)
        ALPHA = 0.5
        SLOPE = 0.2

        def _gat_conv(x, W, a_src, a_dst, b, src, dst):
            n = x.shape[0]
            h = (x @ W).reshape(n, H, C_OUT)
            e_src = jnp.sum(h * a_src[None], -1)
            e_dst = jnp.sum(h * a_dst[None], -1)
            e = jax.nn.leaky_relu(e_src[src] + e_dst[dst], SLOPE)
            m = jax.ops.segment_max(e, dst, num_segments=n)
            ex = jnp.exp(e - m[dst])
            denom = jax.ops.segment_sum(ex, dst, num_segments=n)
            att = ex / denom[dst]
            msg = h[src] * att[:, :, None]
            out = jax.ops.segment_sum(msg, dst, num_segments=n)
            return out.reshape(n, H * C_OUT) + b
        n = x.shape[0]
        loops = jnp.arange(n, dtype=edge_index.dtype)
        src = jnp.concatenate([edge_index[0], loops])
        dst = jnp.concatenate([edge_index[1], loops])
        src_t = jnp.concatenate([edge_index[1], loops])
        dst_t = jnp.concatenate([edge_index[0], loops])
        out_fwd = _gat_conv(x, W1, a_src1, a_dst1, b1, src, dst)
        out_bwd = _gat_conv(x, W2, a_src2, a_dst2, b2, src_t, dst_t)
        return (1.0 - ALPHA) * out_fwd + ALPHA * out_bwd
    edge_index = jnp.stack([src, dst])
    h = jnp.maximum(_layernorm(x, axis=-1), 0.0)
    x = x + _L0_gnn_ref(h, edge_index, edge_weight, L0_gnn_reaction_features, L0_gnn_W, L0_gnn_att, L0_gnn_bias, L0_gnn_gamma, L0_gnn_beta)
    h = jnp.maximum(_layernorm(x, axis=-1), 0.0)
    x = x + _L1_gnn_ref(h, edge_index, L1_gnn_mW1, L1_gnn_mb1, L1_gnn_mW2, L1_gnn_mb2, L1_gnn_uW1, L1_gnn_ub1, L1_gnn_uW2, L1_gnn_ub2)
    h = jnp.maximum(_layernorm(x, axis=-1), 0.0)
    x = x + _L2_gnn_ref(h, src, dst, L2_gnn_W_src, L2_gnn_b_src, L2_gnn_W_dst, L2_gnn_b_dst, L2_gnn_W1a, L2_gnn_W1b, L2_gnn_b1, L2_gnn_W2, L2_gnn_b2, L2_gnn_W3, L2_gnn_b3, L2_gnn_ln_g, L2_gnn_ln_b, L2_gnn_Wg1a, L2_gnn_Wg1b, L2_gnn_bg1, L2_gnn_Wg2, L2_gnn_bg2, L2_gnn_W_out, L2_gnn_b_out)
    h = jnp.maximum(_layernorm(x, axis=-1), 0.0)
    x = x + _L3_gnn_ref(h, edge_index, L3_gnn_W1, L3_gnn_a_src1, L3_gnn_a_dst1, L3_gnn_b1, L3_gnn_W2, L3_gnn_a_src2, L3_gnn_a_dst2, L3_gnn_b2)
    return x

_drawn_inputs = setup_inputs


def setup_inputs(seed=0):
    import zlib

    import numpy as np

    out = dict(_drawn_inputs(seed))
    spreads = {'L0_gnn_bias': (0.0, 0.1),
     'L0_gnn_gamma': (1.0, 0.2),
     'L0_gnn_beta': (0.0, 0.1),
     'L2_gnn_ln_g': (1.0, 0.2),
     'L2_gnn_ln_b': (0.0, 0.1)}
    factors = {}
    for name, (base, spread) in spreads.items():
        noise = np.random.default_rng([zlib.crc32(name.encode()), seed]).standard_normal(out[name].shape)
        drawn = base * np.exp(spread * noise) if base else spread * noise
        out[name] = jnp.asarray(drawn.astype(out[name].dtype))
    for name, factor in factors.items():
        out[name] = (out[name] * factor).astype(out[name].dtype)
    return out
```

```python
from contextlib import ExitStack

import numpy as np
import concourse.bass as bass
from concourse import mybir

F32 = mybir.dt.float32
I32 = mybir.dt.int32
BF16 = mybir.dt.bfloat16
ALU = mybir.AluOpType
ACT = mybir.ActivationFunctionType
AX = mybir.AxisListType

N = 6250
K = 106250
D = 128
RF = 3125
NB = 49
P0, C0 = 125, 850
TC = 10
NG = 220
NT = 4 * NG
U = 8
BIG = 1e30
TINY = 1e-37
EPS = 1e-5
TW = 132
GROUPS = [(b, min(4, NB - b)) for b in range(0, NB, 4)]


def build(nc, a, out):
    ctx = ExitStack()
    dram = lambda n, s, d=F32: nc.dram_tensor(n, s, d, kind="Internal").ap()
    sb = lambda n, s, d=F32: ctx.enter_context(nc.sbuf_tensor(n, s, d))
    sem = lambda n: ctx.enter_context(nc.semaphore(n))

    with ctx:
        recd = [dram(f"recd{o}", (128 * NT, 4)) for o in range(2)]
        tab = {w: dram(f"tab{w}", (NB * 128, w)) for w in (TW, 128, 256)}
        stab = dram("stab", (NB * 128, 4))

        X = sb("X", [128, NB, D])
        H = sb("H", [128, NB, D])
        ACC = sb("ACC", [128, NB, 133])
        B2 = sb("B2", [128, NB * 260])
        REC = sb("REC", [128, 2, NT, 4])
        IDX = sb("IDX", [128, 3, NT], I32)
        MX = sb("MX", [128, NB, 4])
        NV = sb("NV", [128, NB, 12])
        WT = sb("WT", [128, 1400])
        WK = sb("WK", [128, 8800])
        ident = sb("ident", [128, 128])
        iof = sb("iof", [128, 128])
        STG = sb("STG", [128, 4, 4], I32)
        PS = ctx.enter_context(nc.psum_tensor("PS", [128, 8, 512], F32))

        BLK = REC[:, :, :, 3].bitcast(I32)

        ENG = {"pe": nc.tensor, "dve": nc.vector, "act": nc.scalar, "pool": nc.gpsimd, "sp": nc.sync}
        prog = {k: [] for k in ENG}

        class Count:

            def __init__(self, name):
                self.sem, self.at = sem(name), 0

        bar = Count("bar")
        chain_c = [Count(f"ch{i}") for i in range(4)]
        chain_d = [Count(f"cd{i}") for i in range(4)]

        def barrier():
            bar.at += 5
            goal = bar.at
            for e in ENG:
                def f(eng, goal=goal, e=e, landed=[(c.sem, c.at) for c in chain_d if c.at]):
                    if e == "sp":
                        for s_, v_ in landed:
                            eng.wait_ge(s_, v_)
                    eng.drain().then_inc(bar.sem, 1)
                    eng.wait_ge(bar.sem, goal)
                prog[e].append(f)

        def chains(gens):
            lists = [list(g) for g in gens]
            lanes = [[] for _ in range(min(len(lists), 4))]
            for i, l in enumerate(lists):
                lanes[i % len(lanes)] += l
            for n in range(max(len(l) for l in lanes)):
                for i, l in enumerate(lanes):
                    if n >= len(l):
                        continue
                    e, fn = l[n]
                    cc, cd = chain_c[i], chain_d[i]
                    wc, wd = cc.at, cd.at
                    if e == "sp":
                        k = fn(None)
                        cd.at += 16 * k
                    else:
                        cc.at += 1

                    def f(eng, e=e, fn=fn, cc=cc, cd=cd, wc=wc, wd=wd):
                        if wc:
                            eng.wait_ge(cc.sem, wc)
                        if wd:
                            eng.wait_ge(cd.sem, wd)
                        if e == "sp":
                            fn(lambda o, i_: eng.dma_start(o, i_, allow_slow_non_contiguous=True).then_inc(cd.sem, 16))
                        else:
                            fn(eng).then_inc(cc.sem, 1)
                    prog[e].append(f)

        def dmas(pairs):
            def fn(start):
                if start is not None:
                    for o, i in pairs:
                        start(o, i)
                return len(pairs)
            return ("sp", fn)

        def op(e, name, *args, **kw):
            return (e, lambda eng: call(eng, name)(*args, **kw))

        def call(eng, name):
            return {
                "tensor_tensor": lambda *x, **k: eng.tensor_tensor(*x, **k),
                "tensor_scalar": lambda *x, **k: eng.tensor_scalar(*x, **k),
                "tensor_copy": lambda *x, **k: eng.tensor_copy(*x, **k),
                "stt": lambda *x, **k: eng.scalar_tensor_tensor(*x, **k),
                "memset": lambda *x, **k: eng.memset(*x, **k),
                "reduce": lambda *x, **k: eng.tensor_reduce(*x, **k),
                "recip": lambda *x, **k: eng.reciprocal(*x, **k),
                "act": lambda *x, **k: eng.activation(*x, **k),
                "scan": lambda *x, **k: eng.tensor_tensor_scan(*x, **k),
                "iota": lambda *x, **k: eng.iota(*x, **k),
                "affine": lambda *x, **k: eng.affine_select(**k),
                "matmul": lambda *x, **k: eng.matmul(*x, **k),
                "transpose": lambda *x, **k: eng.transpose(*x, **k),
                "bn_stats": lambda *x, **k: eng.bn_stats(*x, **k),
                "bn_aggr": lambda *x, **k: eng.bn_aggr(*x, **k),
            }[name]

        def many(e, calls):
            def fn(eng):
                for name, args, kw in calls:
                    last = call(eng, name)(*args, **kw)
                return last
            return (e, fn)

        def row(v):
            return v.rearrange("(o d) -> o d", o=1)

        OBV = [X, H, ACC]
        ob_at = []
        o, j = 0, 0
        CH = C0 // TC
        W1C = NB * TC // 2
        caps = [NB * 128, NB * 128, NB * 133, 3000]
        flats = [t[:, :, :].rearrange("p b d -> p (b d)") for t in OBV] + [WK[:, 5600:8600]]
        for ch in range(CH):
            if o + W1C > caps[j]:
                o, j = 0, j + 1
            ob_at.append(flats[j][0:P0, o:o + W1C].bitcast(BF16))
            o += W1C
        b2 = B2
        srci = b2[0:P0, 0:850].bitcast(I32)
        dsti = b2[0:P0, 850:1700].bitcast(I32)
        lowi = b2[0:P0, 1700:2550].bitcast(I32)
        blki = b2[0:P0, 2550:3400].bitcast(I32)
        blkf = b2[0:P0, 3400:4250]
        posf = b2[0:P0, 4250:5100]
        posi = b2[0:P0, 5100:5950].bitcast(I32)
        t1i = b2[0:P0, 5950:6800].bitcast(I32)
        sti = b2[0:P0, 6800:7650]
        rec = b2[0:P0, 7650:7650 + 3400].rearrange("p (t f) -> p t f", f=4)
        ew = WK[0:P0, 0:850]
        T_ = WK[0:P0, 1000:1490]
        V_ = [WK[0:P0, 1500 + 500 * i:1990 + 500 * i] for i in range(4)]
        mask = WK[0:P0, 3500:3990]
        cnt = WK[0:P0, 4000:4049]
        cnti = WK[0:P0, 4050:4099].bitcast(I32)
        cnt2 = WK[0:P0, 4100:4149]
        base = [WK[0:P0, 4150 + 50 * i:4199 + 50 * i] for i in range(2)]
        one49 = WK[0:P0, 4300:4349]
        zer = WK[0:P0, 4350:4360]
        IN_ = [WK[0:P0, 4400 + 500 * i:4890 + 500 * i] for i in range(2)]
        LT = WK[0:P0, 5400:5464].bitcast(BF16)
        ON = WK[0:P0, 5500:5564].bitcast(BF16)
        dfl = REC[:, 0, :, :]

        first = [
            op("pool", "iota", iof[:, :], [[1, 128]], base=0, channel_multiplier=0,
               allow_small_or_imprecise_dtypes=True),
            op("pool", "memset", ident[:, :], 0.0),
            op("pool", "affine", out=ident[:, :], in_=ident[:, :], compare_op=ALU.not_equal, fill=1.0,
               base=0, pattern=[[-1, 128]], channel_multiplier=1),
            op("dve", "memset", LT[:, :], 0.0),
            op("pool", "affine", out=LT[:, 0:P0], in_=LT[:, 0:P0], compare_op=ALU.is_gt, fill=-1.0,
               base=0, pattern=[[1, P0]], channel_multiplier=-1),
            op("dve", "memset", ON[:, :], 1.0),
            op("dve", "memset", mask, 1.0),
            op("dve", "memset", mask.rearrange("p (b t) -> p b t", t=TC)[:, :, 0], 0.0),
            op("dve", "memset", one49, 1.0),
            op("dve", "memset", dfl.rearrange("p t f -> p (t f)"), 0.0),
            op("dve", "memset", dfl[:, :, 0], -1.0),
            dmas([(recd[o].rearrange("(p t) f -> p (t f)", p=128), dfl.rearrange("p t f -> p (t f)"))
                  for o in range(2)]),
            dmas([(srci, a["src"].rearrange("(p t) -> p t", p=P0)),
                  (dsti, a["dst"].rearrange("(p t) -> p t", p=P0)),
                  (ew, a["edge_weight"].rearrange("(p t) -> p t", p=P0))]),
        ]
        chains([first])
        barrier()

        c_ob, c_mm, c_v, c_w, c_x, c_y = (Count(n) for n in ("c_ob", "c_mm", "c_v", "c_w", "c_x", "c_y"))
        s_sc = Count("s_sc")

        for o in range(2):
            key, oth = (dsti, srci) if o == 0 else (srci, dsti)
            chains([[
                op("dve", "tensor_scalar", lowi, key, 127, None, ALU.bitwise_and),
                op("dve", "tensor_scalar", blki, key, 7, None, ALU.arith_shift_right),
                op("dve", "tensor_copy", blkf, blki),
                op("dve", "tensor_copy", rec[:, :, 0], lowi),
                op("dve", "tensor_copy", rec[:, :, 1].bitcast(I32), oth),
                op("dve", "tensor_copy", rec[:, :, 2], ew),
                op("dve", "tensor_copy", rec[:, :, 3].bitcast(I32), blki),
            ]])
            barrier()
            a_ob, a_mm, a_v = c_ob.at, c_mm.at, c_v.at

            def f(eng):
                for ch in range(CH):
                    eng.tensor_tensor(
                        ob_at[ch].rearrange("p (b t) -> p b t", t=TC),
                        blkf[:, ch * TC:ch * TC + TC].unsqueeze(1).broadcast_to([P0, NB, TC]),
                        iof[0:P0, 0:NB].unsqueeze(2).broadcast_to([P0, NB, TC]),
                        ALU.is_equal).then_inc(c_ob.sem, 1)
            prog["dve"].append(f)

            def f(eng, a_ob=a_ob):
                for ch in range(CH):
                    eng.wait_ge(c_ob.sem, a_ob + ch + 1)
                    mm = eng.matmul(PS[0:P0, 0, 0:490], ON[:, 0:P0], ob_at[ch], start=(ch == 0), stop=(ch == CH - 1))
                mm.then_inc(c_mm.sem, 1)
            prog["pe"].append(f)
            c_ob.at += CH
            c_mm.at += 1
            barrier()
            chains([[
                op("dve", "reduce", cnt, PS[0:P0, 0, 0:490].rearrange("p (b t) -> p b t", t=TC), AX.X, ALU.add),
                op("dve", "tensor_scalar", cnt2, cnt, 127.0, None, ALU.add),
                op("dve", "tensor_copy", cnti, cnt2),
                op("dve", "tensor_scalar", cnti, cnti, 7, None, ALU.arith_shift_right),
                op("dve", "tensor_copy", cnt2, cnti),
                op("dve", "tensor_scalar", cnt2, cnt2, 128.0, None, ALU.mult),
                op("dve", "scan", cnt, one49, cnt2, 0.0, ALU.mult, ALU.add),
                op("dve", "tensor_tensor", base[0], cnt, cnt2, ALU.subtract),
            ]])
            barrier()
            a_mm, a_v, a_x = c_mm.at, c_v.at, c_x.at

            def f(eng, a_v=a_v):
                for ch in range(CH):
                    if ch >= 2:
                        eng.wait_ge(c_v.sem, a_v + ch - 1)
                    q = 2 * (ch % 2)
                    eng.matmul(PS[0:P0, q, 0:490], LT[:, 0:P0], ob_at[ch], start=True, stop=True)
                    eng.matmul(PS[0:P0, q + 1, 0:490], ON[:, 0:P0], ob_at[ch], start=True,
                               stop=True).then_inc(c_mm.sem, 1)
            prog["pe"].append(f)

            def f(eng, a_mm=a_mm, a_x=a_x):
                x = a_x
                for ch in range(CH):
                    q = 2 * (ch % 2)
                    bt = lambda v: v.rearrange("p (b t) -> p b t", t=TC)
                    eng.wait_ge(c_mm.sem, a_mm + ch + 1)
                    I_ = IN_[ch % 2]
                    eng.tensor_tensor_scan(I_, mask, PS[0:P0, q + 1, 0:490], 0.0, ALU.mult,
                                           ALU.add).then_inc(c_x.sem, 1)
                    eng.wait_ge(c_x.sem, x + 1)
                    eng.tensor_tensor(base[(ch + 1) % 2], base[ch % 2], bt(I_)[:, :, TC - 1],
                                      ALU.add).then_inc(c_x.sem, 1)
                    eng.tensor_tensor(V_[0], PS[0:P0, q, 0:490], I_, ALU.add).then_inc(c_x.sem, 1)
                    eng.wait_ge(c_x.sem, x + 3)
                    eng.tensor_tensor(bt(V_[1]), bt(V_[0]), base[ch % 2].unsqueeze(2).broadcast_to([P0, NB, TC]),
                                      ALU.add).then_inc(c_x.sem, 1)
                    eng.wait_ge(c_x.sem, x + 4)
                    eng.tensor_tensor(V_[2], V_[1], ob_at[ch], ALU.mult).then_inc(c_x.sem, 1)
                    eng.wait_ge(c_x.sem, x + 5)
                    eng.tensor_reduce(posf[:, ch * TC:ch * TC + TC], V_[2].rearrange("p (b t) -> p t b", t=TC),
                                      AX.X, ALU.add).then_inc(c_v.sem, 1)
                    x += 5
            prog["dve"].append(f)
            c_mm.at += CH
            c_v.at += CH
            c_x.at += 5 * CH
            barrier()
            chains([[
                op("dve", "tensor_copy", posi, posf),
                op("dve", "tensor_scalar", t1i, posi, 7, None, ALU.arith_shift_right),
                op("dve", "tensor_scalar", posi, posi, 127, None, ALU.bitwise_and),
                op("dve", "tensor_copy", posf, posi),
                op("dve", "tensor_copy", sti, t1i),
                op("dve", "stt", posf, posf, float(NT), sti, ALU.mult, ALU.add),
                op("dve", "tensor_copy", posi, posf),
            ]])
            barrier()

            def f(eng, o=o, goal=s_sc.at + 16 * C0):
                for t in range(C0):
                    eng.indirect_dma_start(
                        out=recd[o], out_offset=bass.IndirectOffsetOnAxis(ap=posi[:, t:t + 1], axis=0),
                        in_=rec[:, t, :], in_offset=None).then_inc(s_sc.sem, 16)
                eng.wait_ge(s_sc.sem, goal)
            prog["pool"].append(f)
            s_sc.at += 16 * C0
            barrier()
            steps = [
                dmas([(REC[:, o, :, :].rearrange("p t f -> p (t f)"),
                       recd[o].rearrange("(p t) f -> p (t f)", p=128))]),
                op("dve", "tensor_copy", IDX[:, o, :], REC[:, o, :, 1].bitcast(I32)),
            ]
            if o == 1:
                steps.append(op("dve", "tensor_scalar", IDX[:, 2, :], REC[:, 1, :, 1].bitcast(I32),
                                RF - 1, None, ALU.min))
            chains([steps])
            barrier()

        def run_pipeline(stages):
            for e, list_ in stages.items():
                L = max(lag for lag, _ in list_)
                j0 = -(-(L + 8) // U) * U
                j1 = NG // U * U

                def f(eng, list_=list_, L=L, j0=j0, j1=j1):
                    def step(j, u):
                        for lag, fn in list_:
                            if isinstance(j, int) and not 0 <= j - lag < NG:
                                continue
                            fn(eng, j - lag, (u - lag) % U)
                    for j in range(j0):
                        step(j, j % U)
                    with eng.Fori(j0 // U, j1 // U) as i:
                        for u in range(U):
                            step(i * U + u, u)
                    for j in range(j1, NG + L):
                        step(j, j % U)
                prog[e].append(f)

        P = {n: Count("p_" + n) for n in ("ix", "oh", "pt", "ot", "sv", "e", "ex", "r", "ag", "u", "x", "m",
                                          "zt", "h1", "p2", "h2", "p3", "z3", "mv", "th", "rs", "gf")}
        PG_ = [Count(f"p_g{r}") for r in range(4)]

        def blocks(eng, o, g):
            _, v = nc.values_load_multi_w_load_instructions(
                BLK[0:1, o, bass.ds(g * 4, 4)], engines=[eng.engine], min_val=0, max_val=NB - 1,
                skip_runtime_bounds_check_because="node numbers are below 6250, so blocks are below 49")
            return v

        def begin():
            return {n: c.at for n, c in P.items()}, [c.at for c in PG_]

        def end(counts):
            for n, k in counts.items():
                P[n].at += k * NG
            for c in PG_:
                c.at += 64 * (NG // 4)

        def wait(eng, n, at, g, ahead=1, k=1):
            if isinstance(g, int) and g + ahead <= 0:
                return
            eng.wait_ge(P[n].sem, (g + ahead) * k + at[n])

        def gather(idx, table, G, at, last):
            def numbers(eng, g, r):
                wait(eng, last, at, g, -3)
                wait(eng, "gf", at, g, 0)
                eng.tensor_copy(STG[:, r % 4, :], IDX[:, idx, sl(None, g)]).then_inc(P["gf"].sem, 1)

            def rows(eng, g, r):
                if isinstance(g, int):
                    wait(eng, "gf", at, g, 1)
                for k in range(4):
                    eng.indirect_dma_start(
                        out=G[:, r % 4, k, :], out_offset=None, in_=table,
                        in_offset=bass.IndirectOffsetOnAxis(ap=STG[:, r % 4, k:k + 1], axis=0)
                    ).then_inc(PG_[r % 4].sem, 16)
            return [(0, numbers), (1, rows)]

        def gathered(eng, g, r, atg):
            if isinstance(g, int):
                eng.wait_ge(PG_[r % 4].sem, atg[r % 4] + 64 * (g // 4 + 1))
            else:
                eng.wait_ge(PG_[r % 4].sem, (g - r % 4) * 16 + (64 + atg[r % 4]))

        def sl(t, g, n=4):
            return slice(g * n, g * n + n) if isinstance(g, int) else bass.ds(g * n, n)

        def low(o, g):
            return REC[:, o, sl(None, g), 0].unsqueeze(2).broadcast_to([128, 4, 128])

        io4 = iof[:, :].unsqueeze(1).broadcast_to([128, 4, 128])

        def onehot(o, OH, cmp, at, free):
            def fn(eng, g, r):
                wait(eng, free, at, g, -7)
                eng.tensor_tensor(OH[:, r, :, :], io4, low(o, g), cmp).then_inc(P["oh"].sem, 1)
            return fn

        def pe_t(OH, at, bank):
            def fn(eng, g, r):
                wait(eng, "oh", at, g)
                wait(eng, "ot", at, g, -len(bank) + 1)
                for k in range(4):
                    t = eng.transpose(PS[:, bank[r % len(bank)], 128 * k:128 * k + 128], OH[:, r, k, :], ident[:, :])
                t.then_inc(P["pt"].sem, 1)
            return fn

        def act_ot(OT, at, bank):
            def fn(eng, g, r):
                wait(eng, "pt", at, g)
                wait(eng, "sv", at, g, -1)
                eng.activation(OT[:, r % 2, :], PS[:, bank[r % len(bank)], :], ACT.Copy).then_inc(P["ot"].sem, 1)
            return fn

        def pe_sv(o, OT, SELF, W, SV, at, free, nbuf):
            def fn(eng, g, r):
                v = blocks(eng, o, g)
                wait(eng, "ot", at, g)
                wait(eng, free, at, g, -nbuf + 1)
                for k in range(4):
                    mm = eng.matmul(SV(r, k), OT[:, r % 2, 128 * k:128 * k + 128],
                                    SELF[:, bass.ds(v[k] * W, W)], start=True, stop=True)
                mm.then_inc(P["sv"].sem, 1)
            return fn

        def pe_ag(OH, R, W, AG, at, nbuf):
            def fn(eng, g, r):
                wait(eng, "r", at, g)
                wait(eng, "x", at, g, -nbuf + 1, 4)
                for k in range(4):
                    mm = eng.matmul(AG(r, k), OH[:, r, k, :], R[:, r % 2, k, 0:W], start=True, stop=True)
                mm.then_inc(P["ag"].sem, 1)
            return fn

        def dve_u(o, W, AG, at):
            accf = ACC[:, :, :].rearrange("p b d -> p (b d)")

            def fn(eng, g, r):
                v = blocks(eng, o, g)
                wait(eng, "ag", at, g)
                for k in range(4):
                    d = accf[:, bass.ds(v[k] * 133, W)]
                    wait(eng, "x", at, g * 4 + k, 0)
                    eng.tensor_tensor(d, d, AG(r, k), ALU.add).then_inc(P["x"].sem, 1)
            return fn

        wk = [0]

        def work(*shape, dt=F32):
            n = int(np.prod(shape))
            v = WK[:, wk[0]:wk[0] + n]
            wk[0] += n
            assert wk[0] <= 8800, wk[0]
            if len(shape) > 1:
                names = "abcd"[:len(shape)]
                v = v.rearrange("p (" + " ".join(names) + ") -> p " + " ".join(names),
                                **{names[i]: shape[i] for i in range(1, len(shape))})
            return v

        def max_pass(o, Hn):
            wk[0] = 0
            G = work(4, 4, 4)
            OH = work(8, 4, 128)
            XR = work(2, 4 * Hn, 128) if Hn == 1 else work(1, 4 * Hn, 128)
            TM = work(2, 4, Hn)
            nx = 2 if Hn == 1 else 1
            at, atg = begin()
            mxf = MX[:, :, :].rearrange("p b h -> p (b h)")

            def act_x(eng, g, r):
                gathered(eng, g, r, atg)
                wait(eng, "oh", at, g)
                wait(eng, "pt", at, g, -nx + 1)
                for k in range(4):
                    for h in range(Hn):
                        i = eng.activation(XR[:, r % nx, k * Hn + h, :], OH[:, r, k, :], ACT.Identity,
                                           bias=G[:, r % 4, k, h:h + 1], scale=-BIG)
                i.then_inc(P["e"].sem, 1)

            def pe(eng, g, r):
                wait(eng, "e", at, g)
                wait(eng, "m", at, g, -1)
                for k in range(4):
                    for h in range(Hn):
                        q = k * Hn + h
                        bank = (r % 2) * Hn + q // 4
                        t = eng.transpose(PS[:, bank, 128 * (q % 4):128 * (q % 4) + 128], XR[:, r % nx, q, :],
                                          ident[:, :])
                t.then_inc(P["pt"].sem, 1)

            def dve_m(eng, g, r):
                wait(eng, "pt", at, g)
                wait(eng, "x", at, g, -1, 4)
                eng.tensor_reduce(
                    TM[:, r % 2, :, :].rearrange("p k h -> p (k h)"),
                    PS[:, (r % 2) * Hn:(r % 2) * Hn + Hn, :].rearrange("p b (q n) -> p (b q) n", n=128),
                    AX.X, ALU.max).then_inc(P["m"].sem, 1)

            def dve_u2(eng, g, r):
                v = blocks(eng, o, g)
                wait(eng, "m", at, g)
                for k in range(4):
                    d = mxf[:, bass.ds(v[k] * 4, Hn)]
                    wait(eng, "x", at, g * 4 + k, 0)
                    eng.tensor_tensor(d, d, TM[:, r % 2, k, :], ALU.max).then_inc(P["x"].sem, 1)

            run_pipeline({
                "pool": gather(o, stab, G, at, "e"),
                "dve": [(4, dve_u2), (3, dve_m), (0, onehot(o, OH, ALU.not_equal, at, "e"))],
                "act": [(1, act_x)],
                "pe": [(2, pe)],
            })
            end({"gf": 1, "oh": 1, "e": 1, "pt": 1, "m": 1, "x": 4})
            barrier()

        def attention_pass(o, idx, kind):
            wk[0] = 0
            Hn = 4 if kind == "gat" else 1
            KS = {"a1": 2, "a2": 1, "gat": 8}[kind]
            WR = {"a1": 130, "a2": 129, "gat": 132}[kind]
            G = work(4, 4, TW)
            OH = work(8, 4, 128)
            OT = work(2, 512)
            R = work(2, 4, 133)
            E = work(2, 4, Hn)
            LR = work(2, 4, Hn)
            DD = work(2, 4, Hn)
            VA = work(2, 4)
            EX = work(4, 4, Hn)
            at, atg = begin()
            SELF = B2[:, 0:NB * KS]
            SV = lambda r, k: PS[:, 2 + r % 2, k * KS:k * KS + KS]
            AG = lambda r, k: PS[:, 4 + 2 * (r % 2) + k // 2, 256 * (k % 2):256 * (k % 2) + WR]
            svv = lambda r, c, n: PS[:, 2 + r % 2, 0:4 * KS].rearrange("p (k s) -> p k s", s=KS)[:, :, c:c + n]

            def d_e(eng, g, r):
                gathered(eng, g, r, atg)
                wait(eng, "sv", at, g)
                wait(eng, "ex", at, g, -1)
                q = r % 2
                n0 = P["e"]
                w = lambda i: eng.wait_ge(n0.sem, g * 4 + (i + at["e"]))
                es = G[:, r % 4, :, 128:128 + Hn]
                t, s = G[:, r % 4, :, 128:129], G[:, r % 4, :, 129:130]
                a0 = es if kind != "a2" else t
                eng.tensor_tensor(E[:, q, :, :], a0, svv(r, 0, Hn), ALU.add).then_inc(n0.sem, 1)
                eng.tensor_scalar(VA[:, q, :], REC[:, o, sl(None, g), 0], 0.0, None, ALU.is_ge).then_inc(n0.sem, 1)
                w(2)
                eng.scalar_tensor_tensor(LR[:, q, :, :], E[:, q, :, :], 0.2, E[:, q, :, :], ALU.mult,
                                         ALU.max).then_inc(n0.sem, 1)
                w(3)
                sh = s if kind == "a2" else svv(r, Hn, Hn)
                eng.tensor_tensor(E[:, q, :, :], LR[:, q, :, :], sh, ALU.subtract).then_inc(n0.sem, 1)
                w(4)
                eng.tensor_tensor(DD[:, q, :, :], E[:, q, :, :], VA[:, q, :].unsqueeze(2).broadcast_to([128, 4, Hn]),
                                  ALU.mult).then_inc(P["p2"].sem, 1)

            def a_ex(eng, g, r):
                wait(eng, "p2", at, g)
                wait(eng, "r", at, g, -3)
                eng.activation(EX[:, r % 4, :, :], DD[:, r % 2, :, :], ACT.Exp).then_inc(P["ex"].sem, 1)

            def d_r(eng, g, r):
                wait(eng, "ex", at, g)
                wait(eng, "ag", at, g, -1)
                q = r % 2
                if kind == "gat":
                    eng.tensor_copy(R[:, q, :, 128:132], EX[:, r % 4, :, :])
                    eng.tensor_tensor(
                        R[:, q, :, 0:128].rearrange("p k (h c) -> p k h c", c=32),
                        G[:, r % 4, :, 0:128].rearrange("p k (h c) -> p k h c", c=32),
                        EX[:, r % 4, :, :].unsqueeze(3).broadcast_to([128, 4, 4, 32]), ALU.mult).then_inc(P["r"].sem, 1)
                    return
                w2 = REC[:, o, sl(None, g), 2]
                if kind == "a1":
                    eng.tensor_copy(R[:, q, :, 128:129], EX[:, r % 4, :, :])
                eng.scalar_tensor_tensor(R[:, q, :, WR - 1], w2, -1.0, w2, ALU.mult, ALU.max)
                eng.tensor_tensor(LR[:, q, :, 0], EX[:, r % 4, :, 0], w2, ALU.mult).then_inc(P["p3"].sem, 1)
                wait(eng, "p3", at, g)
                eng.tensor_tensor(R[:, q, :, 0:128], G[:, r % 4, :, 0:128],
                                  LR[:, q, :, 0:1].broadcast_to([128, 4, 128]), ALU.mult).then_inc(P["r"].sem, 1)

            run_pipeline({
                "pool": gather(idx, tab[TW], G, at, "r"),
                "dve": [(6, dve_u(o, WR, AG, at)), (4, d_r), (3, d_e), (0, onehot(o, OH, ALU.is_equal, at, "ag"))],
                "act": [(3, a_ex), (1, act_ot(OT, at, [0, 1]))],
                "pe": [(5, pe_ag(OH, R, WR, AG, at, 2)), (2, pe_sv(o, OT, SELF, KS, SV, at, "p2", 2)),
                       (1, pe_t(OH, at, [0, 1]))],
            })
            end({"gf": 1, "oh": 1, "pt": 1, "ot": 1, "sv": 1, "e": 4, "p2": 1, "ex": 1, "r": 1, "ag": 1, "x": 4,
                 "p3": 0 if kind == "gat" else 1})
            barrier()

        def l1_pass():
            wk[0] = 0
            G = work(4, 4, 128)
            OH = work(8, 4, 128)
            OT = work(2, 512)
            R = work(2, 4, 133)
            Z = B2[:, 6400:7424].rearrange("p (a b) -> p a b", b=512)
            at, atg = begin()
            SELF = B2[:, 0:NB * 128]
            SV = lambda r, k: PS[:, 2 + r % 2, 128 * k:128 * k + 128]
            AG = lambda r, k: PS[:, 4 + 2 * (r % 2) + k // 2, 256 * (k % 2):256 * (k % 2) + 129]

            def d_z(eng, g, r):
                gathered(eng, g, r, atg)
                wait(eng, "sv", at, g)
                wait(eng, "r", at, g, -1)
                eng.tensor_tensor(Z[:, r % 2, :], PS[:, 2 + r % 2, :], G[:, r % 4, :, :].rearrange("p k d -> p (k d)"),
                                  ALU.add).then_inc(P["e"].sem, 1)

            def a_r(eng, g, r):
                wait(eng, "e", at, g)
                wait(eng, "ag", at, g, -1)
                eng.activation(R[:, r % 2, :, 0:128], Z[:, r % 2, :].rearrange("p (k d) -> p k d", d=128),
                               ACT.Relu).then_inc(P["r"].sem, 1)

            chains([[op("dve", "memset", R[:, :, :, 128], 1.0)]])
            barrier()
            run_pipeline({
                "pool": gather(0, tab[128], G, at, "e"),
                "dve": [(5, dve_u(0, 129, AG, at)), (3, d_z), (0, onehot(0, OH, ALU.is_equal, at, "ag"))],
                "act": [(3, a_r), (1, act_ot(OT, at, [0, 1]))],
                "pe": [(4, pe_ag(OH, R, 129, AG, at, 2)), (2, pe_sv(0, OT, SELF, 128, SV, at, "e", 2)),
                       (1, pe_t(OH, at, [0, 1]))],
            })
            end({"gf": 1, "oh": 1, "pt": 1, "ot": 1, "sv": 1, "e": 1, "r": 1, "ag": 1, "x": 4})
            barrier()

        def l2_pass(W2, W3, Wg2, b2c, b3b, bg2h):
            wk[0] = 0
            OH = work(8, 4, 128)
            OT = work(2, 512)
            R = work(2, 4, 133)
            H2 = work(512)
            Z3 = work(2, 512)
            BN = work(2, 4, 6)
            MV = work(2, 4, 2)
            VE, RS, TH, GW, GT = (work(2, 4) for _ in range(5))
            PW = work(4)
            hf = H[:, :, :].rearrange("p b d -> p (b d)")
            G = hf[:, 0:4096].rearrange("p (r k d) -> p r k d", r=4, k=4)
            Z, HG = hf[:, 4096:5120], hf[:, 5120:6144]
            at, atg = begin()
            SELF = B2[:, 0:NB * 256]
            SV = lambda r, k: PS[:, 1 + k // 2, 256 * (k % 2):256 * (k % 2) + 256]
            svf = PS[:, 1:3, :].rearrange("p b d -> p (b d)")
            ztf = PS[:, 3:5, :].rearrange("p b d -> p (b d)")
            AG = lambda r, k: PS[:, 6 + k // 2, 129 * (k % 2):129 * (k % 2) + 129]
            GL = PS[:, 7, 300:304]

            def d_z(eng, g, r):
                gathered(eng, g, r, atg)
                wait(eng, "sv", at, g)
                wait(eng, "zt", at, g, 0)
                eng.tensor_tensor(Z, svf, G[:, r % 4, :, :].rearrange("p k d -> p (k d)"),
                                  ALU.add).then_inc(P["e"].sem, 1)

            def p_zt(eng, g, r):
                wait(eng, "e", at, g)
                wait(eng, "h1", at, g, 0)
                for c in range(2):
                    for k in range(4):
                        t = eng.transpose(PS[:, 3 + c, 128 * k:128 * k + 128],
                                          Z[:, 256 * k + 128 * c:256 * k + 128 * c + 128], ident[:, :])
                t.then_inc(P["zt"].sem, 1)

            def a_h1(eng, g, r):
                wait(eng, "zt", at, g)
                wait(eng, "p3", at, g, 0)
                eng.activation(HG, ztf, ACT.Gelu).then_inc(P["h1"].sem, 1)

            def p_2(eng, g, r):
                wait(eng, "h1", at, g)
                wait(eng, "z3", at, g, 0)
                eng.matmul(PS[:, 5, :], W2, HG[:, 0:512], start=True, stop=True).then_inc(P["p2"].sem, 1)

            def a_h2(eng, g, r):
                wait(eng, "p2", at, g)
                wait(eng, "p3", at, g, 0)
                eng.activation(H2, PS[:, 5, :], ACT.Gelu, bias=b2c).then_inc(P["h2"].sem, 1)

            def p_3(eng, g, r):
                wait(eng, "h2", at, g)
                wait(eng, "th", at, g, 0)
                wait(eng, "x", at, g, -2, 4)
                for k in range(4):
                    eng.matmul(PS[:, 5, 128 * k:128 * k + 128], H2[:, 128 * k:128 * k + 128], W3, start=True, stop=True)
                for k in range(4):
                    mm = eng.matmul(GL[:, k:k + 1], HG[:, 512 + 128 * k:640 + 128 * k], Wg2, start=True, stop=True)
                mm.then_inc(P["p3"].sem, 1)

            def a_th(eng, g, r):
                wait(eng, "p3", at, g)
                wait(eng, "r", at, g, -1)
                eng.activation(TH[:, r % 2, :], GL, ACT.Tanh, bias=bg2h, scale=0.5).then_inc(P["th"].sem, 1)

            def d_z3(eng, g, r):
                q = r % 2
                wait(eng, "p3", at, g)
                wait(eng, "rs", at, g, -1)
                eng.tensor_tensor(Z3[:, q, :].rearrange("p (k d) -> p k d", d=128),
                                  PS[:, 5, :].rearrange("p (k d) -> p k d", d=128),
                                  b3b.unsqueeze(1).broadcast_to([128, 4, 128]), ALU.add).then_inc(P["z3"].sem, 1)
                wait(eng, "z3", at, g)
                for k in range(4):
                    i = eng.bn_stats(BN[:, q, k, :], Z3[:, q, 128 * k:128 * k + 128])
                i.then_inc(P["m"].sem, 1)
                wait(eng, "m", at, g * 2, 1)
                wait(eng, "th", at, g)
                eng.tensor_scalar(GT[:, q, :], TH[:, q, :], 0.5, 0.5, ALU.mult, ALU.add)
                for k in range(4):
                    i = eng.bn_aggr(MV[:, q, k, :], BN[:, q, k, :])
                i.then_inc(P["m"].sem, 1)
                wait(eng, "m", at, g * 2, 2)
                eng.tensor_scalar(VE[:, q, :], MV[:, q, :, 1], EPS, None, ALU.add).then_inc(P["mv"].sem, 1)

            def q_rs(eng, g, r):
                wait(eng, "mv", at, g)
                wait(eng, "r", at, g, -1)
                eng.tensor_tensor(RS[:, r % 2, :], VE[:, r % 2, :], PW, ALU.pow).then_inc(P["rs"].sem, 1)

            def d_r(eng, g, r):
                q = r % 2
                wait(eng, "rs", at, g)
                wait(eng, "ag", at, g, -1)
                eng.tensor_copy(R[:, q, :, 128], GT[:, q, :])
                eng.tensor_tensor(GW[:, q, :], GT[:, q, :], RS[:, q, :], ALU.mult).then_inc(P["ix"].sem, 1)
                wait(eng, "ix", at, g)
                for k in range(4):
                    i = eng.tensor_scalar(R[:, q, k, 0:128], Z3[:, q, 128 * k:128 * k + 128], MV[:, q, k, 0:1],
                                          GW[:, q, k:k + 1], ALU.subtract, ALU.mult)
                i.then_inc(P["r"].sem, 1)

            ag = pe_ag(OH, R, 129, AG, at, 1)

            def p_ag(eng, g, r):
                if isinstance(g, int):
                    eng.wait_ge(P["th"].sem, at["th"] + min(g + 3, NG))
                else:
                    wait(eng, "th", at, g, 3)
                ag(eng, g, r)

            chains([[op("dve", "memset", PW, -0.5)]])
            barrier()
            run_pipeline({
                "pool": [(6, q_rs)] + gather(0, tab[256], G, at, "e"),
                "dve": [(9, dve_u(0, 129, AG, at)), (7, d_r), (6, d_z3), (3, d_z),
                        (0, onehot(0, OH, ALU.is_equal, at, "ag"))],
                "act": [(6, a_th), (5, a_h2), (4, a_h1), (1, act_ot(OT, at, [0]))],
                "pe": [(6, p_3), (5, p_2), (8, p_ag), (4, p_zt),
                       (2, pe_sv(0, OT, SELF, 256, SV, at, "e", 1)), (1, pe_t(OH, at, [0]))],
            })
            end({"gf": 1, "oh": 1, "pt": 1, "ot": 1, "sv": 1, "e": 1, "zt": 1, "h1": 1, "p2": 1, "h2": 1, "p3": 1,
                 "th": 1, "z3": 1, "m": 2, "mv": 1, "rs": 1, "ix": 1, "r": 1, "ag": 1, "x": 4})
            barrier()

        def bcast(v, n):
            return row(v).broadcast_to([128, n])

        def flat(t):
            return t.rearrange("p b d -> p (b d)")

        def stats(T, n0=0):
            return [
                many("dve", [("bn_stats", (BNN[:, b, :], T[:, b, 0:128]), {}) for b in range(NB)]),
                many("dve", [("bn_aggr", (MVN[:, b, :], BNN[:, b, :]), {}) for b in range(NB)]),
                op("dve", "tensor_scalar", RSN, MVN[:, :, 1], EPS, None, ALU.add),
                op("dve", "memset", PWN, -0.5),
                op("pool", "tensor_tensor", RSN, RSN, PWN, ALU.pow),
            ]

        BNN = WK[:, 8000:8294].rearrange("p (b s) -> p b s", s=6)
        MVN = WK[:, 8300:8398].rearrange("p (b s) -> p b s", s=2)
        RSN, PWN, NMN = WK[:, 8400:8449], WK[:, 8450:8499], WK[:, 8500:8549]
        S1, S2, S3 = WK[:, 8550:8599], WK[:, 8600:8649], WK[:, 8650:8699]

        def norm_relu():
            return stats(X) + [
                op("dve", "stt", NMN, MVN[:, :, 0], -1.0, RSN, ALU.mult, ALU.mult),
                many("act", [("act", (H[:, b, :], X[:, b, :], ACT.Relu),
                              {"bias": NMN[:, b:b + 1], "scale": RSN[:, b:b + 1]}) for b in range(NB)]),
            ]

        def lane_buf(i, n, k=512):
            return WK[:, 2048 * 0 + k * (4 * n + i):k * (4 * n + i) + k]

        def turn(lane, T, b0, n, dst):
            bank = 2 * lane
            return [
                many("pe", [("transpose", (PS[:, bank, 128 * k:128 * k + 128], T(b0 + k), ident[:, :]), {})
                            for k in range(n)]),
                op("act", "act", dst[:, 0:128 * n], PS[:, bank, 0:128 * n], ACT.Copy),
            ]

        def product(lane, n, terms, W):
            calls = []
            for k in range(n):
                for j, (HT, w) in enumerate(terms):
                    calls.append(("matmul", (prod(lane, n, W)[:, k, :], HT[:, 128 * k:128 * k + 128], w),
                                  {"start": j == 0, "stop": j == len(terms) - 1}))
            return many("pe", calls)

        def prod(lane, n, W):
            return PS[:, 2 * lane:2 * lane + 2, :].rearrange("p b (q c) -> p (b q) c", c=256)[:, 0:n, 0:W]

        def lanes(make):
            chains([make(i % 4, b0, n) for i, (b0, n) in enumerate(GROUPS)])
            barrier()

        def rep(v, n):
            return v.unsqueeze(1).broadcast_to([128, n, v.shape[1]])

        def rows_of(table, b0, n, w):
            return table[b0 * 128:(b0 + n) * 128, 0:w].rearrange("(b p) c -> p b c", p=128)

        chains([[
            op("dve", "memset", X[:, NB - 1, :], 0.0),
            dmas([(X[:, b:b + 4, :], rows_of(a["x"], b, 4, 128)) for b in range(0, NB - 1, 4)] + [
                  (X[0:N - (NB - 1) * 128, NB - 1, :], a["x"][(NB - 1) * 128:N, :])]),
        ] + norm_relu()])
        barrier()

        for l in range(2):
            Wc = WT[:, 0:130]
            att = WT[:, 130:132]
            bia, gam, bet = (WT[:, 140 + 128 * i:268 + 128 * i] for i in range(3))
            WTt = lane_buf(0, 0)[:, 0:128]
            RFt = ACC[:, 0:25, 0:128]
            steps = [
                dmas([(Wc[:, 0:128], a["L0_gnn_W"][l]),
                      (att, a["L0_gnn_att"][l].rearrange("(c p) -> p c", p=128)),
                      (bia, bcast(a["L0_gnn_bias"][l], 128)),
                      (gam, bcast(a["L0_gnn_gamma"][l], 128)),
                      (bet, bcast(a["L0_gnn_beta"][l], 128))]),
                op("pe", "transpose", PS[:, 0, 0:128], Wc[:, 0:128], ident[:, :]),
                op("act", "act", WTt, PS[:, 0, 0:128], ACT.Copy),
                op("pe", "matmul", PS[:, 0, 0:2], WTt, att, start=True, stop=True),
                op("dve", "tensor_copy", Wc[:, 128:130], PS[:, 0, 0:2]),
                op("dve", "memset", ACC[:, 24, 0:128], 0.0),
                dmas([(RFt[:, b:b + 4, :], rows_of(a["L0_gnn_reaction_features"], b, 4, 128))
                      for b in range(0, 24, 4)] + [
                      (RFt[0:RF - 24 * 128, 24, :], a["L0_gnn_reaction_features"][24 * 128:RF, :])]),
                op("dve", "memset", flat(NV[:, :, :]), 0.0),
                op("dve", "memset", flat(MX[:, :, :]), -BIG),
            ]
            chains([steps])
            barrier()

            def l0_nodes(i, b0, n):
                HT = lane_buf(i, 0)
                TS = WK[:, 2048 + 4 * TW * i:2048 + 4 * TW * (i + 1)].rearrange("p (b c) -> p b c", c=TW)
                out_ = turn(i, lambda b: H[:, b, :], b0, n, HT) + [
                    op("dve", "memset", flat(TS), 0.0),
                    product(i, n, [(HT, Wc[:, 0:129])], 129),
                    op("dve", "tensor_copy", TS[:, 0:n, 0:129], prod(i, n, 129)),
                    op("dve", "tensor_copy", NV[:, b0:b0 + n, 0], TS[:, 0:n, 128]),
                    dmas([(rows_of(tab[TW], b0, n, TW), TS[:, 0:n, :])]),
                ]
                if b0 < 25:
                    m = min(n, 25 - b0)
                    out_ += turn(i, lambda b: ACC[:, b, 0:128], b0, m, HT) + [
                        product(i, m, [(HT, Wc[:, 129:130])], 1),
                        op("dve", "tensor_copy", NV[:, b0:b0 + m, 4], prod(i, m, 1)[:, :, 0]),
                    ]
                return out_
            lanes(l0_nodes)
            chains([[dmas([(rows_of(stab, 0, NB, 4), NV[:, :, 0:4])])]])
            barrier()
            max_pass(0, 1)
            SF = B2[:, 0:NB * 2].rearrange("p (b c) -> p b c", c=2)
            t_ = NV[:, :, 4]
            chains([[
                op("dve", "tensor_tensor", S1, MX[:, :, 0], t_, ALU.add),
                op("dve", "stt", SF[:, :, 1], S1, 0.2, S1, ALU.mult, ALU.max),
                op("dve", "tensor_copy", SF[:, :, 0], t_),
                op("dve", "tensor_copy", NV[:, :, 5], SF[:, :, 1]),
                op("dve", "memset", flat(ACC[:, :, :]), 0.0),
            ]])
            barrier()
            attention_pass(0, 0, "a1")
            chains([[
                op("dve", "tensor_scalar", S1, ACC[:, :, 128], TINY, None, ALU.max),
                op("dve", "recip", S1, S1),
                op("dve", "tensor_scalar", S2, ACC[:, :, 129], TINY, None, ALU.max),
                op("dve", "recip", S2, S2),
                op("dve", "tensor_scalar", S3, ACC[:, :, 129], 0.0, None, ALU.is_gt),
                op("dve", "tensor_tensor", S2, S2, S3, ALU.mult),
                op("dve", "tensor_tensor", S2, S2, S1, ALU.mult),
                op("dve", "tensor_tensor", S2, S2, S1, ALU.mult),
                op("dve", "tensor_tensor", ACC[:, 0:25, 0:128], ACC[:, 0:25, 0:128],
                   S2[:, 0:25].unsqueeze(2).broadcast_to([128, 25, 128]), ALU.mult),
                op("dve", "tensor_copy", ACC[:, :, 128:130], NV[:, :, 4:6]),
                op("dve", "tensor_copy", B2[:, 0:NB], NV[:, :, 0]),
                dmas([(rows_of(tab[TW], 0, 25, TW), ACC[:, 0:25, 0:TW])]),
                op("dve", "memset", flat(ACC[:, :, :]), 0.0),
            ]])
            barrier()
            attention_pass(1, 2, "a2")
            A = ACC[:, :, 0:128]
            per = lambda v: v.unsqueeze(2).broadcast_to([128, NB, 128])
            chains([[
                op("dve", "tensor_scalar", S2, ACC[:, :, 128], TINY, None, ALU.max),
                op("dve", "recip", S2, S2),
                op("dve", "tensor_scalar", S3, ACC[:, :, 128], 0.0, None, ALU.is_gt),
                op("dve", "tensor_tensor", S2, S2, S3, ALU.mult),
                op("dve", "tensor_tensor", A, A, per(S2), ALU.mult),
                op("dve", "tensor_tensor", A, A, rep(bia, NB), ALU.add),
            ] + stats(ACC) + [
                op("dve", "tensor_tensor", A, A, per(MVN[:, :, 0]), ALU.subtract),
                op("dve", "tensor_tensor", A, A, per(RSN), ALU.mult),
                op("dve", "tensor_tensor", A, A, rep(gam, NB), ALU.mult),
                op("dve", "tensor_tensor", A, A, rep(bet, NB), ALU.add),
                op("dve", "tensor_tensor", A, A, H[:, :, :], ALU.add),
                op("act", "act", H[:, :, :], A, ACT.Tanh),
            ] + ([] if l == 0 else [op("dve", "tensor_tensor", X[:, :, :], X[:, :, :], H[:, :, :], ALU.add)]
                 + norm_relu())])
            barrier()

        w1, w2, u1, u2 = WT[:, 0:256], WT[:, 256:384], WT[:, 384:640], WT[:, 640:768]
        mb1, mb2, ub1, ub2 = (WT[:, 768 + 128 * i:896 + 128 * i] for i in range(4))
        two = lambda v: v.rearrange("(c p) d -> p c d", p=128)
        c2 = lambda v: v.rearrange("p (c d) -> p c d", c=2)
        chains([[
            dmas([(c2(w1), two(a["L1_gnn_mW1"])), (w2, a["L1_gnn_mW2"]), (c2(u1), two(a["L1_gnn_uW1"])),
                  (u2, a["L1_gnn_uW2"])] + [(d, bcast(a["L1_gnn_" + n], 128)) for d, n in
                                            ((mb1, "mb1"), (mb2, "mb2"), (ub1, "ub1"), (ub2, "ub2"))]),
            op("dve", "memset", flat(ACC[:, :, :]), 0.0),
        ]])
        barrier()
        SQ = B2[:, 0:NB * 128].rearrange("p (b c) -> p b c", c=128)

        def l1_nodes(i, b0, n):
            HT, TS = lane_buf(i, 0), lane_buf(i, 1).rearrange("p (b c) -> p b c", c=128)
            return turn(i, lambda b: H[:, b, :], b0, n, HT) + [
                product(i, n, [(HT, w1)], 256),
                op("act", "act", TS[:, 0:n, :], prod(i, n, 256)[:, :, 0:128], ACT.Copy),
                op("dve", "tensor_tensor", SQ[:, b0:b0 + n, :], prod(i, n, 256)[:, :, 128:256], rep(mb1, n), ALU.add),
                dmas([(rows_of(tab[128], b0, n, 128), TS[:, 0:n, :])]),
            ]
        lanes(l1_nodes)
        l1_pass()

        def l1_after(i, b0, n):
            HT, HU, TS = lane_buf(i, 0), lane_buf(i, 1), lane_buf(i, 2).rearrange("p (b c) -> p b c", c=128)
            tb = lambda b: TS[:, b - b0, :]
            return turn(i, lambda b: ACC[:, b, 0:128], b0, n, HT) + [
                product(i, n, [(HT, w2)], 128),
                op("dve", "tensor_tensor", TS[:, 0:n, :], ACC[:, b0:b0 + n, 128:129].broadcast_to([128, n, 128]),
                   rep(mb2, n), ALU.mult),
                op("dve", "tensor_tensor", TS[:, 0:n, :], TS[:, 0:n, :], prod(i, n, 128), ALU.add),
            ] + turn(i, tb, b0, n, HT) + turn(i, lambda b: H[:, b, :], b0, n, HU) + [
                product(i, n, [(HU, u1[:, 0:128]), (HT, u1[:, 128:256])], 128),
                op("dve", "tensor_tensor", TS[:, 0:n, :], prod(i, n, 128), rep(ub1, n), ALU.add),
                op("act", "act", TS[:, 0:n, :], TS[:, 0:n, :], ACT.Relu),
            ] + turn(i, tb, b0, n, HT) + [
                product(i, n, [(HT, u2)], 128),
                op("dve", "tensor_tensor", TS[:, 0:n, :], prod(i, n, 128), rep(ub2, n), ALU.add),
                op("act", "act", TS[:, 0:n, :], TS[:, 0:n, :], ACT.Relu),
                op("dve", "tensor_tensor", X[:, b0:b0 + n, :], X[:, b0:b0 + n, :], TS[:, 0:n, :], ALU.add),
            ]
        lanes(l1_after)
        chains([norm_relu()])
        barrier()

        W2, W3, Wo = WT[:, 0:128], WT[:, 128:256], WT[:, 256:384]
        b3b, gb, bb, bob = (WT[:, 384 + 128 * i:512 + 128 * i] for i in range(4))
        Wg2, b2c, bg2 = WT[:, 896:897], WT[:, 897:898], WT[:, 898:899]
        bsd = WT[:, 900:902]
        raw = [WK[:, 128 * i:128 * i + 128] for i in range(6)]
        Wsd = [WK[:, 768 + 256 * i:1024 + 256 * i] for i in range(2)]
        bsr = [WK[:, 1280 + 256 * i:1536 + 256 * i] for i in range(2)]
        b1g = WK[:, 1792:2048]
        tmp = [WK[:, 2048 + 128 * i:2176 + 128 * i] for i in range(4)]
        col = lambda v: v.rearrange("(p o) -> p o", o=1)
        g = lambda n: a["L2_gnn_" + n]
        steps = [
            dmas([(W2, g("W2")), (W3, g("W3")), (Wo, g("W_out")), (b3b, bcast(g("b3"), 128)),
                  (gb, bcast(g("ln_g"), 128)), (bb, bcast(g("ln_b"), 128)), (bob, bcast(g("b_out"), 128)),
                  (Wg2, g("Wg2")), (b2c, col(g("b2"))), (bg2, bcast(g("bg2"), 1)),
                  (bsd[:, 0:1], col(g("b_src"))), (bsd[:, 1:2], col(g("b_dst"))),
                  (b1g[:, 0:128], bcast(g("b1"), 128)), (b1g[:, 128:256], bcast(g("bg1"), 128)),
                  (raw[0], g("W_src")), (raw[1], g("W_dst")), (raw[2], g("W1a")), (raw[3], g("Wg1a")),
                  (raw[4], g("W1b")), (raw[5], g("Wg1b"))]),
            op("dve", "tensor_scalar", bg2, bg2, 0.5, None, ALU.mult),
            op("dve", "memset", flat(ACC[:, :, :]), 0.0),
        ]
        for i in range(2):
            second = WK[:, 256 + 256 * i:512 + 256 * i]
            steps += [
                op("pe", "transpose", PS[:, 0, 0:128], raw[i], ident[:, :]),
                op("act", "act", tmp[i], PS[:, 0, 0:128], ACT.Copy),
                op("pe", "matmul", PS[:, 0, 0:256], tmp[i], second, start=True, stop=True),
                op("dve", "tensor_copy", Wsd[i], PS[:, 0, 0:256]),
                op("dve", "tensor_copy", tmp[2 + i], bsd[:, i:i + 1].broadcast_to([128, 128])),
                op("pe", "matmul", PS[:, 0, 0:256], tmp[2 + i], second, start=True, stop=True),
                op("dve", "tensor_copy", bsr[i], PS[:, 0, 0:256]),
            ]
        steps.append(op("dve", "tensor_tensor", bsr[1], bsr[1], b1g, ALU.add))
        chains([steps])
        barrier()
        SB = B2[:, 0:NB * 256].rearrange("p (b c) -> p b c", c=256)

        def l2_nodes(i, b0, n):
            HT = WK[:, 2048 + 512 * i:2560 + 512 * i]
            TS = WK[:, 4096 + 960 * 0 + 1024 * i:5120 + 1024 * i].rearrange("p (b c) -> p b c", c=256)
            return turn(i, lambda b: H[:, b, :], b0, n, HT) + [
                product(i, n, [(HT, Wsd[0])], 256),
                op("dve", "tensor_tensor", TS[:, 0:n, :], prod(i, n, 256), rep(bsr[0], n), ALU.add),
                dmas([(rows_of(tab[256], b0, n, 256), TS[:, 0:n, :])]),
                product(i, n, [(HT, Wsd[1])], 256),
                op("dve", "tensor_tensor", SB[:, b0:b0 + n, :], prod(i, n, 256), rep(bsr[1], n), ALU.add),
            ]
        lanes(l2_nodes)
        l2_pass(W2, W3, Wg2, b2c, b3b, bg2)

        def l2_after(i, b0, n):
            HT, TS, TU = (lane_buf(i, j) for j in range(3))
            TS, TU = (v.rearrange("p (b c) -> p b c", c=128) for v in (TS, TU))
            return [
                op("dve", "tensor_tensor", TS[:, 0:n, :], ACC[:, b0:b0 + n, 0:128], rep(gb, n), ALU.mult),
                op("dve", "tensor_tensor", TU[:, 0:n, :], ACC[:, b0:b0 + n, 128:129].broadcast_to([128, n, 128]),
                   rep(bb, n), ALU.mult),
                op("dve", "tensor_tensor", TS[:, 0:n, :], TS[:, 0:n, :], TU[:, 0:n, :], ALU.add),
            ] + turn(i, lambda b: TS[:, b - b0, :], b0, n, HT) + [
                product(i, n, [(HT, Wo)], 128),
                op("dve", "tensor_tensor", TS[:, 0:n, :], prod(i, n, 128), rep(bob, n), ALU.add),
                op("dve", "tensor_tensor", X[:, b0:b0 + n, :], X[:, b0:b0 + n, :], TS[:, 0:n, :], ALU.add),
            ]
        lanes(l2_after)
        chains([norm_relu()])
        barrier()

        HN = B2[:, 400:400 + NB * TW].rearrange("p (b c) -> p b c", c=TW)
        SF = B2[:, 0:NB * 8].rearrange("p (b c) -> p b c", c=8)
        for d in range(2):
            Wc = WT[:, 0:136]
            asd = WT[:, 136:144]
            bo = WT[:, 144:272]
            nm = str(d + 1)
            WTt = lane_buf(0, 0)[:, 0:128]
            ga = lambda n: a["L3_gnn_" + n + nm]
            steps = [
                op("dve", "memset", asd, 0.0),
                dmas([(Wc[:, 0:128], ga("W")), (bo, bcast(ga("b"), 128))]
                     + [(asd[32 * h:32 * h + 32, 4 * j + h:4 * j + h + 1], col(ga(n)[h]))
                        for j, n in enumerate(("a_src", "a_dst")) for h in range(4)]),
                op("pe", "transpose", PS[:, 0, 0:128], Wc[:, 0:128], ident[:, :]),
                op("act", "act", WTt, PS[:, 0, 0:128], ACT.Copy),
                op("pe", "matmul", PS[:, 0, 0:8], WTt, asd, start=True, stop=True),
                op("dve", "tensor_copy", Wc[:, 128:136], PS[:, 0, 0:8]),
                op("dve", "tensor_scalar", bo, bo, 0.5, None, ALU.mult),
            ]
            chains([steps])
            barrier()

            def l3_nodes(i, b0, n):
                HT = lane_buf(i, 0)
                return turn(i, lambda b: H[:, b, :], b0, n, HT) + [
                    product(i, n, [(HT, Wc)], 136),
                    op("dve", "tensor_copy", HN[:, b0:b0 + n, :], prod(i, n, 136)[:, :, 0:132]),
                    op("dve", "tensor_copy", SF[:, b0:b0 + n, 0:4], prod(i, n, 136)[:, :, 132:136]),
                ]
            lanes(l3_nodes)
            chains([[
                dmas([(rows_of(tab[TW], 0, NB, TW), HN), (rows_of(stab, 0, NB, 4), HN[:, :, 128:132])]),
                op("dve", "tensor_copy", MX[:, :, :], HN[:, :, 128:132]),
            ]])
            barrier()
            max_pass(d, 4)
            Q1, Q2 = (WK[:, 200 * j:200 * j + 196].rearrange("p (b c) -> p b c", c=4) for j in range(2))
            chains([[
                op("dve", "tensor_tensor", Q1, MX[:, :, :], SF[:, :, 0:4], ALU.add),
                op("dve", "stt", SF[:, :, 4:8], Q1, 0.2, Q1, ALU.mult, ALU.max),
                op("dve", "tensor_tensor", Q1, HN[:, :, 128:132], SF[:, :, 0:4], ALU.add),
                op("dve", "stt", Q2, Q1, 0.2, Q1, ALU.mult, ALU.max),
                op("dve", "tensor_tensor", Q1, Q2, SF[:, :, 4:8], ALU.subtract),
                op("act", "act", ACC[:, :, 128:132], Q1, ACT.Exp),
            ] + [op("dve", "tensor_tensor", ACC[:, :, 32 * h:32 * h + 32], HN[:, :, 32 * h:32 * h + 32],
                    ACC[:, :, 128 + h:129 + h].broadcast_to([128, NB, 32]), ALU.mult) for h in range(4)]])
            barrier()
            attention_pass(d, d, "gat")
            chains([[
                op("dve", "recip", Q1, ACC[:, :, 128:132]),
                op("dve", "tensor_scalar", Q1, Q1, 0.5, None, ALU.mult),
            ] + [op("dve", "tensor_tensor", ACC[:, :, 32 * h:32 * h + 32], ACC[:, :, 32 * h:32 * h + 32],
                    Q1[:, :, h:h + 1].broadcast_to([128, NB, 32]), ALU.mult) for h in range(4)] + [
                op("dve", "tensor_tensor", X[:, :, :], X[:, :, :], ACC[:, :, 0:128], ALU.add),
                op("dve", "tensor_tensor", X[:, :, :], X[:, :, :], rep(bo, NB), ALU.add),
            ]])
            barrier()
        chains([[dmas([(out[0:(NB - 1) * 128, :].rearrange("(b p) d -> p b d", p=128), X[:, 0:NB - 1, :]),
                       (out[(NB - 1) * 128:N, :], X[0:N - (NB - 1) * 128, NB - 1, :])])]])
        end_c, end_v = chain_d[0], chain_d[0].at
        prog["sp"].append(lambda eng: eng.wait_ge(end_c.sem, end_v))

        block = ctx.enter_context(nc.Block())
        for name, reg in (("sp", block.sync), ("pool", block.gpsimd), ("act", block.scalar),
                          ("pe", block.tensor), ("dve", block.vector)):
            @reg
            def _(eng, name=name):
                for f in prog[name]:
                    f(eng)


def kernel(**inputs):
    import concourse.bacc as bacc
    from concourse.bass_utils import run_bass_kernel_spmd

    nc = bacc.Bacc("TRN2", target_bir_lowering=False, num_devices=1)
    arrays, aps = {}, {}
    for name, v in inputs.items():
        v = np.ascontiguousarray(v)
        arrays["in_" + name] = v
        aps[name] = nc.dram_tensor("in_" + name, v.shape, mybir.dt.from_np(v.dtype), kind="ExternalInput").ap()
    out = nc.dram_tensor("out_0", (N, D), F32, kind="ExternalOutput").ap()
    build(nc, aps, out)
    r = run_bass_kernel_spmd(nc, [arrays], core_ids=[0])
    return r.results[0]["out_0"]
```
